# Optimizing a Trainium2 kernel written in Bass

```python
import numpy as np
import jax
import jax.numpy as jnp

def _softmax(x, axis=-1):
    return jax.nn.softmax(x, axis=axis)

def _gelu(x):
    return jax.nn.gelu(x, approximate=True)

def _silu(x):
    return jax.nn.silu(x)

def _sigmoid(x):
    return jax.nn.sigmoid(x)

def _layernorm(x, axis=-1, eps=1e-05):
    m = jnp.mean(x, axis=axis, keepdims=True)
    v = jnp.var(x, axis=axis, keepdims=True)
    return (x - m) / jnp.sqrt(v + eps)

def _scatter_add(tgt, idx, src, axis=0):
    return tgt.at[idx].add(src)

def _segment_sum(src, seg, n):
    return jax.ops.segment_sum(src, seg, n)
kernel_name = 'mk_gnn_preln_d1_gnn_r32_ac8a52'

def setup_inputs(seed: int=0):
    np.random.seed(seed)
    _w = jnp.asarray

    def _rec_inputs():
        import jax
        import jax.numpy as jnp
        _gk = jax.random.key(seed)
        x = -0.000202 + 1 * jax.random.normal(jax.random.fold_in(_gk, 1), (50000, 128), jnp.float32)
        src = jax.random.randint(jax.random.fold_in(_gk, 2), (25000,), 0, 50000, jnp.int32)
        dst = jnp.minimum((50000 * jax.random.uniform(jax.random.fold_in(_gk, 3), (25000,)) ** 2.0).astype(jnp.int32), 49999)
        _o = jnp.argsort(dst, stable=True)
        src = src[_o]
        dst = dst[_o]
        edge_type_8 = jax.random.randint(jax.random.fold_in(_gk, 13), (25000,), 0, 8, jnp.int32)
        return (x, src, dst, edge_type_8)
    x, src, dst, edge_type_8 = _rec_inputs()

    def _L0_gnn_setup():
        import jax, jax.numpy as jnp
        import numpy as np
        N = 50000
        E = 15625
        R = 8
        IN_DIM = 128
        HID = 128
        OUT = 128
        NUM_GRAPHS = 64
        EPS_BN = 1e-05

        def _glorot(key, shape):
            fan_in, fan_out = (shape[-2], shape[-1])
            lim = np.sqrt(6.0 / (fan_in + fan_out))
            return jax.random.uniform(key, shape, jnp.float32, -lim, lim)

        def rgcn_conv(h, src, dst, etype, W, root, bias):
            seg = dst * R + etype
            msg = h[src]
            agg = jax.ops.segment_sum(msg, seg, num_segments=N * R)
            cnt = jax.ops.segment_sum(jnp.ones((seg.shape[0],), h.dtype), seg, num_segments=N * R)
            agg = agg / jnp.maximum(cnt, 1.0)[:, None]
            agg = agg.reshape(N, R, -1)
            out = jnp.einsum('nri,rio->no', agg, W) + h @ root + bias
            return out

        def batch_norm(h, gamma, beta):
            mu = jnp.mean(h, axis=0, keepdims=True)
            var = jnp.mean((h - mu) ** 2, axis=0, keepdims=True)
            return (h - mu) * jax.lax.rsqrt(var + EPS_BN) * gamma + beta

        def lrelu(h):
            return jax.nn.leaky_relu(h, 0.1)
        key = jax.random.key(seed)
        ks = jax.random.split(key, 24)
        x = jax.random.normal(ks[0], (N, IN_DIM), jnp.float32)
        edge_index = jax.random.randint(ks[1], (2, E), 0, N, jnp.int64)
        edge_type = jax.random.randint(ks[2], (E,), 0, R, jnp.int64)
        batch = jnp.sort(jax.random.randint(ks[3], (N,), 0, NUM_GRAPHS, jnp.int64))
        d = {'x': x, 'edge_index': edge_index, 'edge_type': edge_type, 'batch': batch, 'W1': _glorot(ks[4], (R, IN_DIM, HID)), 'root1': _glorot(ks[5], (IN_DIM, HID)), 'b1': jnp.zeros((HID,), jnp.float32), 'W2': _glorot(ks[6], (R, HID, HID)), 'root2': _glorot(ks[7], (HID, HID)), 'b2': jnp.zeros((HID,), jnp.float32), 'W3': _glorot(ks[8], (R, HID, HID)), 'root3': _glorot(ks[9], (HID, HID)), 'b3': jnp.zeros((HID,), jnp.float32), 'g1': jnp.ones((HID,), jnp.float32), 'beta1': jnp.zeros((HID,), jnp.float32), 'g2': jnp.ones((HID,), jnp.float32), 'beta2': jnp.zeros((HID,), jnp.float32), 'A1': _glorot(ks[10], (HID, HID // 2)), 'a1': jnp.zeros((HID // 2,), jnp.float32), 'A2': _glorot(ks[11], (HID // 2, 1)), 'a2': jnp.zeros((1,), jnp.float32), 'C1': _glorot(ks[12], (2 * HID, HID)), 'c1': jnp.zeros((HID,), jnp.float32), 'C2': _glorot(ks[13], (HID, OUT)), 'c2': jnp.zeros((OUT,), jnp.float32)}
        return d
    _L0_gnn_all = _L0_gnn_setup()
    _L0_gnn_in = {k: v for k, v in _L0_gnn_all.items() if k in ('W1', 'root1', 'b1', 'W2', 'root2', 'b2', 'W3', 'root3', 'b3', 'g1', 'beta1', 'g2', 'beta2', 'A1', 'a1', 'A2', 'a2', 'C1', 'c1', 'C2', 'c2')}
    del _L0_gnn_all
    return {'x': x, 'src': src, 'dst': dst, 'edge_type_8': edge_type_8, 'L0_gnn_W1': _L0_gnn_in['W1'], 'L0_gnn_root1': _L0_gnn_in['root1'], 'L0_gnn_b1': _L0_gnn_in['b1'], 'L0_gnn_W2': _L0_gnn_in['W2'], 'L0_gnn_root2': _L0_gnn_in['root2'], 'L0_gnn_b2': _L0_gnn_in['b2'], 'L0_gnn_W3': _L0_gnn_in['W3'], 'L0_gnn_root3': _L0_gnn_in['root3'], 'L0_gnn_b3': _L0_gnn_in['b3'], 'L0_gnn_g1': _L0_gnn_in['g1'], 'L0_gnn_beta1': _L0_gnn_in['beta1'], 'L0_gnn_g2': _L0_gnn_in['g2'], 'L0_gnn_beta2': _L0_gnn_in['beta2'], 'L0_gnn_A1': _L0_gnn_in['A1'], 'L0_gnn_a1': _L0_gnn_in['a1'], 'L0_gnn_A2': _L0_gnn_in['A2'], 'L0_gnn_a2': _L0_gnn_in['a2'], 'L0_gnn_C1': _L0_gnn_in['C1'], 'L0_gnn_c1': _L0_gnn_in['c1'], 'L0_gnn_C2': _L0_gnn_in['C2'], 'L0_gnn_c2': _L0_gnn_in['c2']}

def reference(x, src, dst, edge_type_8, L0_gnn_W1, L0_gnn_root1, L0_gnn_b1, L0_gnn_W2, L0_gnn_root2, L0_gnn_b2, L0_gnn_W3, L0_gnn_root3, L0_gnn_b3, L0_gnn_g1, L0_gnn_beta1, L0_gnn_g2, L0_gnn_beta2, L0_gnn_A1, L0_gnn_a1, L0_gnn_A2, L0_gnn_a2, L0_gnn_C1, L0_gnn_c1, L0_gnn_C2, L0_gnn_c2):
    import jax
    import jax.numpy as jnp

    def _L0_gnn_ref(x, edge_index, edge_type, batch, W1, root1, b1, W2, root2, b2, W3, root3, b3, g1, beta1, g2, beta2, A1, a1, A2, a2, C1, c1, C2, c2):
        import jax, jax.numpy as jnp
        import numpy as np
        N = 50000
        E = 15625
        R = 8
        IN_DIM = 128
        HID = 128
        OUT = 128
        NUM_GRAPHS = 64
        EPS_BN = 1e-05

        def _glorot(key, shape):
            fan_in, fan_out = (shape[-2], shape[-1])
            lim = np.sqrt(6.0 / (fan_in + fan_out))
            return jax.random.uniform(key, shape, jnp.float32, -lim, lim)

        def rgcn_conv(h, src, dst, etype, W, root, bias):
            seg = dst * R + etype
            msg = h[src]
            agg = jax.ops.segment_sum(msg, seg, num_segments=N * R)
            cnt = jax.ops.segment_sum(jnp.ones((seg.shape[0],), h.dtype), seg, num_segments=N * R)
            agg = agg / jnp.maximum(cnt, 1.0)[:, None]
            agg = agg.reshape(N, R, -1)
            out = jnp.einsum('nri,rio->no', agg, W) + h @ root + bias
            return out

        def batch_norm(h, gamma, beta):
            mu = jnp.mean(h, axis=0, keepdims=True)
            var = jnp.mean((h - mu) ** 2, axis=0, keepdims=True)
            return (h - mu) * jax.lax.rsqrt(var + EPS_BN) * gamma + beta

        def lrelu(h):
            return jax.nn.leaky_relu(h, 0.1)
        src, dst = (edge_index[0], edge_index[1])
        h = rgcn_conv(x, src, dst, edge_type, W1, root1, b1)
        h = lrelu(batch_norm(h, g1, beta1))
        h = rgcn_conv(h, src, dst, edge_type, W2, root2, b2)
        h = lrelu(batch_norm(h, g2, beta2))
        node_emb = rgcn_conv(h, src, dst, edge_type, W3, root3, b3)
        scores = lrelu(node_emb @ A1 + a1) @ A2 + a2
        attn = jax.nn.softmax(scores, axis=0)
        global_emb = jax.ops.segment_sum(node_emb * attn, batch, num_segments=NUM_GRAPHS)
        combined = jnp.concatenate([node_emb, global_emb[batch]], axis=1)
        final = lrelu(combined @ C1 + c1) @ C2 + c2
        norm = jnp.linalg.norm(final, axis=1, keepdims=True)
        return final / jnp.maximum(norm, 1e-12)
    edge_index = jnp.stack([src, dst])
    batch0 = jnp.zeros((50000,), jnp.int32)
    h = jnp.maximum(_layernorm(x, axis=-1), 0.0)
    x = x + _L0_gnn_ref(h, edge_index, edge_type_8, batch0, L0_gnn_W1, L0_gnn_root1, L0_gnn_b1, L0_gnn_W2, L0_gnn_root2, L0_gnn_b2, L0_gnn_W3, L0_gnn_root3, L0_gnn_b3, L0_gnn_g1, L0_gnn_beta1, L0_gnn_g2, L0_gnn_beta2, L0_gnn_A1, L0_gnn_a1, L0_gnn_A2, L0_gnn_a2, L0_gnn_C1, L0_gnn_c1, L0_gnn_C2, L0_gnn_c2)
    return x

_drawn_inputs = setup_inputs


def setup_inputs(seed=0):
    import zlib

    import numpy as np

    out = dict(_drawn_inputs(seed))
    spreads = {'L0_gnn_b1': (0.0, 2.0),
     'L0_gnn_b2': (0.0, 2.0),
     'L0_gnn_b3': (0.0, 2.0),
     'L0_gnn_g1': (1.0, 0.6),
     'L0_gnn_beta1': (0.0, 0.8),
     'L0_gnn_g2': (1.0, 0.6),
     'L0_gnn_beta2': (0.0, 0.8),
     'L0_gnn_a1': (0.0, 2.0),
     'L0_gnn_c1': (0.0, 2.0),
     'L0_gnn_c2': (0.0, 2.0)}
    factors = {'L0_gnn_A1': 4.772, 'L0_gnn_A2': 2.836}
    for name, (base, spread) in spreads.items():
        noise = np.random.default_rng([zlib.crc32(name.encode()), seed]).standard_normal(out[name].shape)
        drawn = base * np.exp(spread * noise) if base else spread * noise
        out[name] = jnp.asarray(drawn.astype(out[name].dtype))
    for name, factor in factors.items():
        out[name] = (out[name] * factor).astype(out[name].dtype)
    return out
```

```python
import concourse.bass as bass
from concourse import mybir
from contextlib import ExitStack

F32 = mybir.dt.float32
I32 = mybir.dt.int32
ALU = mybir.AluOpType
ACT = mybir.ActivationFunctionType
AX = mybir.AxisListType

P = 128
N = 50000
D = 128
E = 25000
R = 8
EPS = 1e-5
SLOPE = 0.1

EP = 125
ET = E // EP

CH = 8
NCH = 26
NT = CH * NCH
RP = NT // 2
SLOTS = NT * P
KEY = 1 << 16
assert EP * ET == E and SLOTS >= E + R * (P - 1) and N < KEY

T = 4
GROUP = P * T
FULL = N // GROUP
TAIL_P, TAIL_T = 112, 3
assert N - FULL * GROUP == TAIL_P * TAIL_T
NG = FULL + 1
GL = FULL // T
assert GL * T == FULL - 1

CONSTS = 21
OFF = 4


def done(n):
    return n + (OFF + 1)


def reuse(n, depth):
    return n + (OFF + 1 - depth)


class Chain:

    def __init__(self, eng, sem):
        self.eng, self.sem, self.n, self.i, self.per = eng, sem, 0, None, 0

    def mark(self, ins):
        ins.then_inc(self.sem, 1)
        self.n += 1
        return self.n

    def wait(self, n=None):
        n = self.n if n is None else n
        self.eng.wait_ge(self.sem, n if self.i is None else self.i * self.per + n)

    def enter(self, i, per, first=0):
        self.i, self.per, self.start = i, per, self.n
        self.first = first
        self.n -= first * per

    def leave(self, times):
        assert self.n + self.first * self.per - self.start == self.per, (self.n, self.start, self.per)
        self.n = self.start + self.per * times
        self.i = None


def gnn_program(nc, t, out):
    ctx = ExitStack()
    with ctx:
        def sb(name, shape, dt=F32):
            return ctx.enter_context(nc.sbuf_tensor(name, shape, dt))

        def pb(name, shape):
            return ctx.enter_context(nc.psum_tensor(name, shape, F32))

        def sem(name):
            return ctx.enter_context(nc.semaphore(name))

        nodes_a = nc.dram_tensor("nodes_a", (N + SLOTS, D), F32).ap()
        nodes_b = nc.dram_tensor("nodes_b", (N + SLOTS, D), F32).ap()
        records = nc.dram_tensor("records", (SLOTS + 2, 2), I32).ap()
        heads = nc.dram_tensor("heads", (RP, 2 * P), F32).ap()
        headkey = nc.dram_tensor("headkey", (RP, 2), F32).ap()
        hidden = nc.dram_tensor("hidden", (NG, P, GROUP), F32).ap()
        table = {1: nodes_a, 2: nodes_b, 3: nodes_a}

        ident = sb("ident", [P, P])
        iota = sb("iota", [P, P])
        ones = sb("ones", [P, P])
        before = sb("before", [P, P])
        W = {l: sb(f"W{l}_sb", [P, R * D]) for l in (1, 2, 3)}
        root = {l: sb(f"root{l}_sb", [P, D]) for l in (1, 2, 3)}
        brow = {l: sb(f"brow{l}", [P, D]) for l in (1, 2, 3)}
        grow = {l: sb(f"grow{l}", [P, D]) for l in (1, 2)}
        betarow = {l: sb(f"betarow{l}", [P, D]) for l in (1, 2)}
        A1 = sb("A1_sb", [P, D // 2])
        a1 = sb("a1_sb", [D // 2, 1])
        A2 = sb("A2_sb", [D // 2, 1])
        A2rep = sb("A2rep", [D // 2, P])
        a2 = sb("a2_sb", [P, 1])
        C1 = sb("C1_sb", [P, 2, D])
        c1 = sb("c1_sb", [P, 1])
        C2 = sb("C2_sb", [P, D])
        c2row = sb("c2row", [P, D])

        M = sb("M", [P, NT, D])
        MF = M[:, :, :].rearrange("p j d -> p (j d)")
        G = sb("G", [P, 2 * CH, D])
        S = sb("S", [P, 2, CH, P])
        HT = sb("HT", [P, 2, T * P])
        lnst = sb("lnst", [P, CH, 6])
        lnmv = sb("lnmv", [P, 2, CH, 2])
        lnsd = sb("lnsd", [P, 2, CH])
        lnr = sb("lnr", [P, 2, CH])
        lnb = sb("lnb", [P, 2, CH])
        srcA = sb("srcA", [P, NT], I32)
        toA = sb("toA", [P, NT], I32)
        repA = sb("repA", [P, NT])
        invA = sb("invA", [P, NT])
        woff = sb("woff", [1, NT], I32)
        same = sb("same", [1, NT], I32)
        other = sb("other", [1, NT], I32)
        idx = sb("idx", [P, 2, CH], I32)
        stage = sb("stage", [P, 2, CH, D])
        fixS = sb("fixS", [RP, 2, 2, RP])
        fixto = sb("fixto", [RP, 2], I32)
        fixin = sb("fixin", [RP, 2 * P])
        fixrow = sb("fixrow", [RP, 2, D])

        X = sb("X", [P, T, GROUP])
        O = sb("O", [P, T, GROUP])
        hrow = sb("hrow", [P, 2, GROUP])
        hpre = sb("hpre", [P, 2, GROUP])
        hT = sb("hT", [P, 2, GROUP])
        hsum = sb("hsum", [P, NG])
        xst = sb("xst", [P, 2, T, 6])
        xmv = sb("xmv", [P, 2, T, 2])
        xr = sb("xr", [P, 2, T])
        xsd = sb("xsd", [P, 2, T])
        eps = sb("eps", [P, 1])
        hbar = sb("hbar", [P, 1])
        hbarw = sb("hbarw", [P, P])
        mean = sb("mean", [P, D])
        tmp = sb("tmp", [P, D])
        tmp2 = sb("tmp2", [P, D])
        var = sb("var", [P, D])
        scale = sb("scale", [P, D])
        shift = sb("shift", [P, D])
        scol = sb("scol", [P, 1])
        bcol = sb("bcol", [P, 1])

        gmax = sb("gmax", [P, NG])
        nbias = sb("nbias", [P, NG])
        esum = sb("esum", [P, NG])
        wsum = sb("wsum", [P, NG])
        small = sb("small", [P, 16])
        nrm = sb("nrm", [P, T, T])
        nr2 = sb("nr2", [P, T, T])
        nrm2 = sb("nrm2", [P, T, T])

        def part(p, first, size, dt=F32):
            ap = MF[0:p, first:first + size]
            return ap if dt == F32 else ap.bitcast(dt)

        src_i = part(EP, 0, ET, I32)
        dst_i = part(EP, ET, ET, I32)
        typ_i = part(EP, 2 * ET, ET, I32)
        typ_f = part(EP, 3 * ET, ET)
        dst_f = part(EP, 4 * ET, ET)
        pos_f = part(EP, 5 * ET, ET)
        term = part(EP, 6 * ET, ET)
        posI = part(EP, 7 * ET, ET, I32)
        recE = part(EP, 8 * ET, 2 * ET, I32).rearrange("p (t two) -> p t two", two=2)
        hot = part(EP, 10 * ET, R * ET).rearrange("p (r t) -> p r t", r=R)
        run = part(EP, 18 * ET, R * ET).rearrange("p (r t) -> p r t", r=R)
        z0 = part(EP, 26 * ET, ET)
        b0 = 27 * ET
        pad_i = part(P, b0, 2 * NT + 4, I32)
        b0 += 2 * NT + 4
        rowtot = part(EP, b0, R)
        tot = part(P, b0 + 8, R)
        toti = part(P, b0 + 16, R, I32)
        tbase = part(P, b0 + 24, R)
        offs = part(EP, b0 + 32, R)
        recst = part(EP, b0 + 48, 2 * CH * 2, I32).rearrange("p (s k two) -> p s k two", s=2, two=2)
        b0 += 48 + 4 * CH
        L2 = 2 * P
        names = ["keyR", "srcR", "prevR", "nextR", "slotR", "firstR", "rs", "re", "tsR", "realR", "w0", "w1", "repR", "invR", "toR", "dstR", "nf"]
        v = {}
        for nm in names:
            v[nm] = part(RP, b0, L2)
            b0 += L2
        rec3 = [part(RP, b0 + 2 * L2 * k, 2 * L2, I32).rearrange("p (s two) -> p s two", two=2) for k in range(3)]
        b0 += 6 * L2
        keyi = part(RP, b0, L2, I32)
        lowi = part(RP, b0 + L2, L2, I32)
        b0 += 2 * L2
        tr = part(1, b0, 4 * P)
        trow = part(1, b0 + 4 * P, 4 * NT)
        trowi = part(1, b0 + 4 * P + 4 * NT, NT, I32)
        b0 += 4 * P + 5 * NT
        ca = part(RP, b0, 16)
        b0 += 16
        fk = part(RP, b0, 2)
        fv = part(RP, b0 + 2, 2)
        jR = part(RP, b0 + 4, 2)
        frep = part(RP, b0 + 6, 2)
        fk2 = part(RP, b0 + 8, 8)
        b0 += 16
        fkall = part(P, b0, NT)
        jall = part(P, b0 + NT, NT)
        fe = part(RP, b0 + 2 * NT, 2 * NT).rearrange("p (h j) -> p h j", h=2)
        b0 += 4 * NT
        assert b0 <= NT * D, b0

        psT = [pb(f"psT{k}", [P, GROUP]) for k in range(2)]
        psO = [pb(f"psO{k}", [P, GROUP]) for k in range(2)]
        psH = [pb(f"psH{k}", [P, GROUP]) for k in range(2)]
        psM = [pb(f"psM{k}", [P, GROUP]) for k in range(2)]

        consts_in = sem("consts_in")
        edges_in = sem("edges_in")
        made = sem("made")
        spare0 = sem("spare0")
        pads_made = sem("pads_made")
        pads_in = sem("pads_in")
        x_in = [sem(f"x_in{k}") for k in range(T)]
        o_ready = sem("o_ready")
        o_stored = [sem(f"o_stored{k}") for k in range(T)]
        hrow_ready = sem("hrow_ready")
        t_done = sem("t_done")
        pre_ready = sem("pre_ready")
        hT_ready = sem("hT_ready")
        root_done = sem("root_done")
        gath = [sem(f"gath{k}") for k in range(2)]
        g_ready = sem("g_ready")
        ln_ready = sem("ln_ready")
        s_ready = sem("s_ready")
        h_done = sem("h_done")
        h_out = sem("h_out")
        m_done = sem("m_done")
        m_out = sem("m_out")
        staged = sem("staged")
        scat = [sem(f"scat{k}") for k in range(2)]
        heads_out = sem("heads_out")
        heads_in = sem("heads_in")
        fix_done = sem("fix_done")
        fix_ready = sem("fix_ready")
        fixed = sem("fixed")
        msum_done = sem("msum_done")
        hbar_ready = sem("hbar_ready")
        mean_ready = sem("mean_ready")
        cen_ready = sem("cen_ready")
        sq_ready = sem("sq_ready")
        sq_used = sem("sq_used")
        bn_rows = sem("bn_rows")
        ss_ready = sem("ss_ready")
        col_done = sem("col_done")
        bn_ready = sem("bn_ready")
        pos_ready = sem("pos_ready")
        tot_ready = sem("tot_ready")
        tot_done = sem("tot_done")
        rec_in = sem("rec_in")
        car_ready = sem("car_ready")
        car_done = sem("car_done")
        car2_ready = sem("car2_ready")
        car2_done = sem("car2_done")
        slot_ready = sem("slot_ready")
        slot_done = sem("slot_done")
        slot_out = sem("slot_out")
        hk_ready = sem("hk_ready")
        hk_stored = sem("hk_stored")
        hk_in = sem("hk_in")
        edges_ready = sem("edges_ready")
        a_done = sem("a_done")
        z_ready = sem("z_ready")
        s1_ready = sem("s1_ready")
        sc_done = sem("sc_done")
        q_done = sem("q_done")
        q_out = sem("q_out")
        max_ready = sem("max_ready")
        e_ready = sem("e_ready")
        w_done = sem("w_done")
        q_stored = [sem(f"q_stored{k}") for k in range(2)]
        pool_ready = sem("pool_ready")
        pool_done = sem("pool_done")
        qb_ready = sem("qb_ready")
        q_in = [sem(f"q_in{k}") for k in range(T)]
        f_pre = sem("f_pre")
        f_ready = sem("f_ready")
        f_done = sem("f_done")
        fin_ready = sem("fin_ready")
        nrm_ready = sem("nrm_ready")
        pool_chain = sem("pool_chain")
        act_chain = sem("act_chain")
        dve_chain = sem("dve_chain")
        xv_ready = sem("xv_ready")
        xs_ready = sem("xs_ready")
        lnv_ready = sem("lnv_ready")
        lns_ready = sem("lns_ready")
        var_ready = sem("var_ready")
        sd_ready = sem("sd_ready")
        nsd_ready = sem("nsd_ready")
        passed = sem("passed")
        seen = sem("seen")

        def rows(tab, g, tail=False):
            if tail:
                return tab[FULL * GROUP:N, :].rearrange("(p t) d -> p (t d)", t=TAIL_T)
            return tab[bass.ds(g * GROUP, GROUP), :].rearrange("(p t) d -> p (t d)", t=T)

        def inner(ap, tail):
            return ap[0:TAIL_P, 0:TAIL_T * D] if tail else ap

        def cols(ap, tail):
            ap = ap.rearrange("f (t n) -> f t n", t=T)
            return ap[:, 0:TAIL_T, 0:TAIL_P] if tail else ap

        def four(ap):
            return ap.rearrange("p (t d) -> p t d", t=T)

        def rep4(ap):
            return ap[:, :].unsqueeze(1).to_broadcast([P, T, D])

        PASS = {"root1": 0, "stat1": 1, "root2": 2, "stat2": 3, "root3": 4, "pool": 5, "last": 6}
        USES = [len(range(k, NG, T)) for k in range(T)]

        def x_value(name, g, k):
            return (PASS[name] * USES[k]) * 16 + 16 + g[0] * 16

        READ = {"root1": (hrow_ready, 0), "stat1": (cen_ready, 0), "root2": (t_done, NG), "stat2": (cen_ready, NG),
                "root3": (t_done, 2 * NG), "pool": (t_done, 3 * NG), "last": (o_ready, 3 * NG)}
        ORDER = ["root1", "stat1", "root2", "stat2", "root3", "pool", "last"]

        def scat_base(l, k):
            return 16 * CH * ((13 if k == 0 else 12) + (l - 1) * (NCH // 2))

        def loop_group(i, k):
            return (i, k, i * T + k, False)

        LAST = [(GL, 0, GL * T, False), (GL, 1, FULL, True)]

        def QR(k):
            return G[:, T * k:T * k + T, :].rearrange("p a b -> p (a b)")

        def place(n, k):
            return MF[:, (T * n + k) * GROUP:(T * n + k + 1) * GROUP]

        def embT(k):
            return place(0, k)

        def EX(k):
            return place(1, k)

        def FIN(k):
            return place(2, k)

        def S1(k):
            return place(3, k)[0:D // 2, :]

        def X4(s):
            return place(4, s)

        block = ctx.enter_context(nc.Block())

        def o_value(name, g, k):
            n = {"root1": 0, "root2": 1, "root3": 2, "last": 3}[name]
            return (1 + n * USES[k]) * 16 + g[0] * 16

        ROOT = {"root1": 0, "root2": 1, "root3": 2, "last": 3}

        def pipeline(eng, stages, chain=None, per=0):
            lags = [lag for _, lag in stages]

            def step(n):
                for body, lag in stages:
                    g = n + lag
                    if 0 <= g < NG:
                        body((g // T, g % T, g, g == NG - 1))
            for n in range(-max(lags), T):
                step(n)
            with eng.Fori(1, GL - 1) as i:
                if chain:
                    chain.enter(i, per * T, first=1)
                for k in range(T):
                    for body, lag in stages:
                        di, dk = divmod(k + lag, T)
                        body((i + di, dk, i * T + (k + lag), False))
                if chain:
                    chain.leave(GL - 2)
            for n in range((GL - 1) * T, NG - min(lags)):
                step(n)

        @block.sync
        def _(sp):
            for dst_ap, name in ((src_i, "src"), (dst_i, "dst"), (typ_i, "edge_type_8")):
                sp.dma_start(dst_ap, t[name].rearrange("(p t) -> p t", t=ET)).then_inc(edges_in, 16)
            consts = []
            for l in (1, 2, 3):
                consts.append((W[l][:, :].rearrange("i (r o) -> i r o", r=R), t[f"L0_gnn_W{l}"].rearrange("r i o -> i r o")))
                consts.append((root[l][:, :], t[f"L0_gnn_root{l}"]))
                consts.append((brow[l][:, :], t[f"L0_gnn_b{l}"].partition_broadcast(P)))
            for l in (1, 2):
                consts.append((grow[l][:, :], t[f"L0_gnn_g{l}"].partition_broadcast(P)))
                consts.append((betarow[l][:, :], t[f"L0_gnn_beta{l}"].partition_broadcast(P)))
            consts.append((A1[:, :], t["L0_gnn_A1"]))
            consts.append((a1[:, :], t["L0_gnn_a1"].rearrange("(p o) -> p o", o=1)))
            consts.append((A2[:, :], t["L0_gnn_A2"]))
            consts.append((a2[:, :], t["L0_gnn_a2"].partition_broadcast(P)))
            consts.append((C1[:, :, :], t["L0_gnn_C1"].rearrange("(h i) o -> i h o", h=2)))
            consts.append((c1[:, :], t["L0_gnn_c1"].rearrange("(p o) -> p o", o=1)))
            consts.append((C2[:, :], t["L0_gnn_C2"]))
            consts.append((c2row[:, :], t["L0_gnn_c2"].partition_broadcast(P)))
            assert len(consts) == CONSTS
            for a, b in consts:
                sp.dma_start(a, b).then_inc(consts_in, 16)

            sp.wait_ge(pads_made, 1)
            sp.dma_start(records[0:SLOTS, :].rearrange("(p s) two -> p (s two)", p=P), pad_i[:, 0:2 * NT]).then_inc(pads_in, 16)
            sp.dma_start(records[SLOTS:SLOTS + 2, :].rearrange("(o s) two -> o (s two)", o=1), pad_i[0:1, 0:4]).then_inc(pads_in, 16)
            sp.wait_ge(spare0, 1)
            zr = SLOTS // T
            for k in range(T):
                for tab in ((nodes_a,), (nodes_b,))[k % 2]:
                    lo = N + (k // 2) * (SLOTS // 2)
                    sp.dma_start(tab[lo:lo + SLOTS // 2, :].rearrange("(p a t) d -> p a (t d)", p=P, t=T),
                                 O[:, k:k + 1, :].to_broadcast([P, SLOTS // 2 // P // T, GROUP])).then_inc(o_stored[k], 16)

            def load(name, tab, g):
                k = g[1]
                read, base = READ[name]
                sp.wait_ge(read, reuse(g[2] + base, T))
                sp.dma_start(inner(X[:, k, :], g[3]), rows(tab, g[2], g[3])).then_inc(x_in[k], 16)

            def store(name, tab, g):
                k = g[1]
                sp.wait_ge(o_ready, done(ROOT[name] * NG + g[2]))
                sp.dma_start(rows(tab, g[2], g[3]), inner(O[:, k, :], g[3])).then_inc(o_stored[k], 16)

            def start_pass(name):
                if name != "root1":
                    read, base = READ[ORDER[ORDER.index(name) - 1]]
                    sp.wait_ge(read, done(base + NG - 1))

            def node_pass(name, tab_in, tab_out, extra=None):
                start_pass(name)
                stages = [(lambda g: load(name, tab_in, g), 3)]
                if extra:
                    stages.append((extra, 3))
                if tab_out is not None:
                    stages.append((lambda g: store(name, tab_out, g), 0))
                pipeline(nc.sync, stages)

            node_pass("root1", t["x"], nodes_a)
            sp.wait_ge(scat[0], scat_base(1, 0))
            sp.wait_ge(scat[1], scat_base(1, 1))
            for k in range(3):
                sp.dma_start(rec3[k], records[k:k + SLOTS, :].rearrange("(q s) two -> q s two", s=L2)).then_inc(rec_in, 16)
            sp.wait_ge(hk_ready, 1)
            sp.dma_start(headkey, fk2[:, 0:2]).then_inc(hk_stored, 16)
            sp.wait_ge(hk_stored, 16)
            sp.dma_start(fkall, headkey.rearrange("q h -> (q h)").partition_broadcast(P)).then_inc(hk_in, 16)

            for l in (1, 2, 3):
                if l > 1:
                    node_pass(f"root{l}", table[l - 1], table[l])
                sp.wait_ge(m_out, done(2 * NCH * l - 1))
                sp.dma_start(heads.rearrange("(o q) s -> o q s", o=1), MF[0:1, :].rearrange("o (q s) -> o q s", s=2 * P)).then_inc(heads_out, 16)
                sp.wait_ge(heads_out, 16 * l)
                sp.dma_start(fixin[:, :], heads).then_inc(heads_in, 16)
                for k in range(2):
                    sp.wait_ge(scat[k], scat_base(l + 1, k))
                sp.wait_ge(fixed, 32 * l)
                if l < 3:
                    node_pass(f"stat{l}", table[l], None)

            def store_q(g):
                sp.wait_ge(q_out, done(g[2]))
                sp.dma_start(hidden[bass.ds(g[2], 1), :, :].rearrange("g f n -> (g f) n"), hpre[:, g[1] % 2, :]).then_inc(q_stored[g[1] % 2], 16)

            start_pass("pool")
            pipeline(nc.sync, [(lambda g: load("pool", nodes_a, g), 3), (store_q, 0)])
            sp.wait_ge(q_stored[0], 16 * (NG // 2))
            sp.wait_ge(q_stored[1], 16 * (NG // 2))

            def load_q(g):
                sp.wait_ge(f_pre, reuse(g[2], T))
                sp.dma_start(QR(g[1]), hidden[bass.ds(g[2], 1), :, :].rearrange("g f n -> (g f) n")).then_inc(q_in[g[1]], 16)

            sp.wait_ge(qb_ready, 1)
            node_pass("last", t["x"], out, extra=load_q)
            for k in range(T):
                sp.wait_ge(o_stored[k], (1 + 4 * USES[k]) * 16)

        @block.gpsimd
        def _(pool):
            ch = Chain(pool, pool_chain)
            pool.memset(ident[:, :], 0.0)
            pool.memset(eps[:, :], EPS).then_inc(made, 1)
            pool.memset(ones[:, :], 1.0)
            ch.mark(pool.memset(before[:, :], 1.0))
            nc.gpsimd.iota(iota[:, :], pattern=[[1, P]], base=0, channel_multiplier=0, allow_small_or_imprecise_dtypes=True).then_inc(made, 1)
            nc.gpsimd.iota(v["slotR"], pattern=[[1, L2]], base=0, channel_multiplier=L2, allow_small_or_imprecise_dtypes=True).then_inc(made, 1)
            nc.gpsimd.iota(jR, pattern=[[1, 2]], base=0, channel_multiplier=2, allow_small_or_imprecise_dtypes=True).then_inc(made, 1)
            nc.gpsimd.iota(jall, pattern=[[1, NT]], base=0, channel_multiplier=0, allow_small_or_imprecise_dtypes=True).then_inc(made, 1)
            ch.wait()
            nc.gpsimd.affine_select(out=ident[:, :], in_=ident[:, :], compare_op=ALU.not_equal, fill=1.0,
                                    base=0, pattern=[[-1, P]], channel_multiplier=1).then_inc(made, 1)
            nc.gpsimd.affine_select(out=before[:, :], in_=before[:, :], compare_op=ALU.is_gt, fill=0.0,
                                    base=0, pattern=[[1, P]], channel_multiplier=-1).then_inc(made, 1)

            pool.wait_ge(pos_ready, 1)
            pool.wait_ge(pads_in, 32)

            def sort_chunk(c, n, s):
                if c is not s:
                    pool.wait_ge(scat[s], n * (16 * CH))
                    pool.sem_inc(seen)
                ch.mark(nc.gpsimd.tensor_copy(idx[0:EP, s, :], posI[:, bass.ds(c * CH, CH)]))
                ch.mark(nc.gpsimd.tensor_copy(recst[:, s, :, :], recE[:, bass.ds(c * CH, CH), :]))
                ch.wait()
                pool.sem_inc(seen)
                for k in range(CH):
                    pool.indirect_dma_start(out=records[:, :], out_offset=bass.IndirectOffsetOnAxis(ap=idx[0:EP, s, k:k + 1], axis=0),
                                            in_=recst[:, s, k, :], in_offset=None).then_inc(scat[s], 16)

            NE = ET // CH
            for s in range(2):
                sort_chunk(s, 0, s)
            with nc.gpsimd.Fori(1, NE // 2) as i:
                ch.enter(i, 4, first=1)
                for s in range(2):
                    sort_chunk(i * 2 + s, i, s)
                ch.leave(NE // 2 - 1)
            sort_chunk(NE - 1, NE // 2, 0)

            pool.wait_ge(edges_ready, 1)

            def gather_chunk(l, c, n, s, tab):
                pool.wait_ge(h_done, reuse(2 * NCH * (l - 1) + c * 2 + 1, 4))
                pool.sem_inc(seen)
                ch.mark(nc.gpsimd.tensor_copy(idx[:, s, :], srcA[:, bass.ds(c * CH, CH)]))
                ch.wait()
                pool.sem_inc(seen)
                for k in range(CH):
                    pool.indirect_dma_start(out=G[:, s * CH + k, :], out_offset=None, in_=tab[:, :],
                                            in_offset=bass.IndirectOffsetOnAxis(ap=idx[:, s, k:k + 1], axis=0)).then_inc(gath[s], 16)

            def scatter_chunk(l, c, n, s, tab):
                for k in range(CH):
                    pool.wait_ge(staged, done(NT * (l - 1) + c * CH + k))
                    pool.sem_inc(seen)
                    if k == 0:
                        ch.mark(nc.gpsimd.tensor_copy(idx[:, s, :], toA[:, bass.ds(c * CH, CH)]))
                        ch.wait()
                        pool.sem_inc(seen)
                    pool.indirect_dma_start(out=tab[:, :], out_offset=bass.IndirectOffsetOnAxis(ap=idx[:, s, k:k + 1], axis=0),
                                            in_=stage[:, s, k, :], in_offset=None, compute_op=ALU.add).then_inc(scat[s], 16)

            for l in (1, 2, 3):
                with nc.gpsimd.Fori(0, NCH // 2) as i:
                    ch.enter(i, 2)
                    for s in range(2):
                        gather_chunk(l, i * 2 + s, i, s, t["x"] if l == 1 else table[l - 1])
                    ch.leave(NCH // 2)
                for k in range(T):
                    pool.wait_ge(o_stored[k], (1 + l * USES[k]) * 16)
                for k in range(2):
                    pool.wait_ge(gath[k], 16 * CH * (NCH // 2) * l)
                with nc.gpsimd.Fori(0, NCH // 2) as i:
                    ch.enter(i, 2)
                    for s in range(2):
                        scatter_chunk(l, i * 2 + s, i, s, table[l])
                    ch.leave(NCH // 2)
                for k in range(2):
                    pool.wait_ge(scat[k], scat_base(l + 1, k))
                pool.wait_ge(fix_ready, l)
                for h in range(2):
                    pool.indirect_dma_start(out=table[l][:, :], out_offset=bass.IndirectOffsetOnAxis(ap=fixto[:, h:h + 1], axis=0),
                                            in_=fixrow[:, h, :], in_offset=None, compute_op=ALU.add).then_inc(fixed, 16)
                pool.wait_ge(fixed, 32 * l)

        @block.scalar
        def _(act):
            ch = Chain(act, act_chain)
            for s_ in (pre_ready, h_out, m_out, staged, sq_ready, q_out, f_pre, z_ready, e_ready, ss_ready,
                       xs_ready, lns_ready, nsd_ready):
                act.sem_inc(s_, OFF)
            act.wait_ge(consts_in, 16 * CONSTS)

            def evac_t(name, g):
                n = ROOT[name] * NG + g[2]
                s = g[1] % 2
                act.wait_ge(t_done, done(n))
                if name == "root1":
                    act.wait_ge(root_done, reuse(n, 2))
                    nc.scalar.activation(cols(hT[:, s, :], g[3]), cols(psT[s][:, :], g[3]), ACT.Relu,
                                         accum_out=hsum[:, bass.ds(g[2], 1)]).then_inc(hT_ready, 1)
                else:
                    act.wait_ge(hT_ready, reuse(n, 2))
                    nc.scalar.activation(cols(hpre[:, s, :], g[3]), cols(psT[s][:, :], g[3]), ACT.Identity,
                                         scale=scol[:, 0:1], bias=bcol[:, 0:1]).then_inc(pre_ready, 1)

            def evac_h(l, c, b):
                n = 2 * NCH * (l - 1) + c * 2 + b
                act.wait_ge(h_done, done(n))
                act.wait_ge(m_done, reuse(n, 2))
                nc.scalar.activation(HT[:, b, :], psH[b][:, :], ACT.Copy).then_inc(h_out, 1)

            def evac_m(l, c, b):
                n = 2 * NCH * (l - 1) + c * 2 + b
                act.wait_ge(m_done, done(n))
                nc.scalar.activation(MF[:, bass.ds(c * (CH * D) + b * (T * D), T * D)], psM[b][:, :], ACT.Copy).then_inc(m_out, 1)

            def relu_g(l, c, s):
                act.wait_ge(lnv_ready, done(c))
                nc.scalar.activation(lnsd[:, s, :], lnmv[:, s, :, 1], ACT.Sqrt, bias=eps[:, 0:1]).then_inc(lns_ready, 1)
                act.wait_ge(ln_ready, done(c))
                for k in range(CH):
                    last = nc.scalar.activation(G[:, s * CH + k, :], G[:, s * CH + k, :], ACT.Relu,
                                                scale=lnr[:, s, k:k + 1], bias=lnb[:, s, k:k + 1])
                last.then_inc(g_ready, 1)

            def std_x(g):
                act.wait_ge(xv_ready, done(g[2]))
                nc.scalar.activation(xsd[:, g[1] % 2, :], xmv[:, g[1] % 2, :, 1], ACT.Sqrt, bias=eps[:, 0:1]).then_inc(xs_ready, 1)

            act.wait_ge(made, 7)
            pipeline(nc.scalar, [(std_x, 2), (lambda g: evac_t("root1", g), 0)])

            for n, (h, dst_ap) in enumerate([(h, a) for a in (srcA, toA, repA, invA) for h in range(2)]):
                act.wait_ge(slot_done, n + 1)
                nc.scalar.activation(dst_ap[:, h:NT:2], psT[n % 2][:, 0:RP], ACT.Copy).then_inc(slot_out, 1)

            for l in (1, 2, 3):
                if l == 1:
                    with nc.scalar.Fori(0, NCH // 2) as i:
                        for s in range(2):
                            c = i * 2 + s
                            relu_g(1, c, s)
                            for b in range(2):
                                evac_h(1, c, b)
                            for b in range(2):
                                evac_m(1, c, b)
                else:
                    act.wait_ge(bn_ready, l - 1)

                    def chunk(c, groups):
                        for n, step in enumerate(("t", "t", "h0", "t", "m0", "t", "h1", "m1")):
                            if step == "t":
                                if groups:
                                    evac_t(f"root{l}", groups.pop(0))
                            elif step[0] == "h":
                                evac_h(l, c, int(step[1]))
                            else:
                                evac_m(l, c, int(step[1]))

                    with nc.scalar.Fori(0, GL // 2) as i:
                        for s in range(2):
                            c = i * 2 + s
                            chunk(c, [(c, k, c * T + k, False) for k in range(T)])
                    chunk(GL, [LAST[0]])
                    chunk(GL + 1, [LAST[1]])

                act.wait_ge(m_out, done(2 * NCH * l - 1))
                with nc.scalar.Fori(0, NCH // 2) as i:
                    for s in range(2):
                        for k in range(CH):
                            j = i * (2 * CH) + (s * CH + k)
                            more = nc.scalar.value_load(same[0:1, bass.ds(j, 1)], min_val=0, max_val=16 * CH)
                            more2 = nc.scalar.value_load(other[0:1, bass.ds(j, 1)], min_val=0, max_val=16 * CH)
                            act.wait_ge(scat[s], i * (16 * CH) + more + scat_base(l, s))
                            act.wait_ge(scat[1 - s], i * (16 * CH) + more2 + (scat_base(l, 1 - s) + (0 if s else -16 * CH)))
                            nc.scalar.activation(stage[:, s, k, :], MF[:, bass.ds(j * D, D)], ACT.Copy).then_inc(staged, 1)

                for h in range(2):
                    act.wait_ge(fix_done, 2 * (l - 1) + h + 1)
                    last = nc.scalar.activation(fixrow[:, h, :], psT[h][0:RP, 0:D], ACT.Copy)
                last.then_inc(fix_ready, 1)

                if l < 3:
                    def square(g):
                        n = (l - 1) * NG + g[2]
                        act.wait_ge(cen_ready, done(n))
                        act.wait_ge(sq_used, reuse(n, 2))
                        nc.scalar.activation(hpre[:, g[1] % 2, :], hrow[:, g[1] % 2, :], ACT.Square).then_inc(sq_ready, 1)
                    pipeline(nc.scalar, [(square, 0)])
                    act.wait_ge(var_ready, l)
                    nc.scalar.activation(tmp2[:, :], var[:, :], ACT.Sqrt).then_inc(sd_ready, 1)

            act.wait_ge(root_done, done(3 * NG - 1))
            act.wait_ge(hT_ready, done(3 * NG - 1))

            def pool_t(g):
                act.wait_ge(t_done, done(g[2] + 3 * NG))
                act.wait_ge(q_done, reuse(g[2], 4))
                act.wait_ge(w_done, reuse(g[2], 4))
                nc.scalar.activation(embT(g[1]), psT[g[1] % 2][:, :], ACT.Copy).then_inc(hT_ready, 1)

            def pool_z(g):
                act.wait_ge(a_done, done(g[2]))
                act.wait_ge(s1_ready, reuse(g[2], 2))
                nc.scalar.activation(hrow[0:D // 2, g[1] % 2, :], psO[g[1] % 2][0:D // 2, :], ACT.Identity, bias=a1[:, 0:1]).then_inc(z_ready, 1)

            def pool_q(g):
                s = g[1] % 2
                act.wait_ge(q_done, done(g[2]))
                if not (isinstance(g[2], int) and g[2] < 2):
                    act.wait_ge(q_stored[s], g[0] * 32 + (0 if g[1] < 2 else 16))
                nc.scalar.activation(hpre[:, s, :], psM[s][:, :], ACT.Copy).then_inc(q_out, 1)

            def pool_e(g):
                act.wait_ge(max_ready, done(g[2]))
                act.wait_ge(w_done, reuse(g[2], 4))
                nc.scalar.activation(cols(EX(g[1]), g[3]), cols(psH[g[1] % 2][:, :], g[3]), ACT.Exp, bias=nbias[:, bass.ds(g[2], 1)],
                                     accum_out=esum[:, bass.ds(g[2], 1)]).then_inc(e_ready, 1)

            pipeline(nc.scalar, [(pool_t, 1), (pool_z, 0), (pool_q, 0), (pool_e, -2)])

            act.wait_ge(pool_ready, 1)
            nc.scalar.activation(hsum[:, :], gmax[:, :], ACT.Exp, bias=small[:, 0:1]).then_inc(pool_done, 1)

            act.wait_ge(qb_ready, 1)

            def last_q(g):
                act.wait_ge(q_in[g[1]], g[0] * 16 + 16)
                act.wait_ge(f_ready, reuse(g[2], 2))
                nc.scalar.activation(hpre[:, g[1] % 2, :], QR(g[1]), ACT.Identity, bias=small[:, 4:5]).then_inc(f_pre, 1)

            def last_s(g):
                act.wait_ge(fin_ready, done(g[2]))
                act.wait_ge(o_ready, reuse(g[2] + 3 * NG, 4))
                for k in range(T):
                    last = nc.scalar.activation(X4(g[1] % 2)[:, k * D:(k + 1) * D], FIN(g[1])[:, k * D:(k + 1) * D], ACT.Square,
                                                accum_out=nrm[:, g[1], k:k + 1])
                last.then_inc(ss_ready, 1)

            def last_r(g):
                act.wait_ge(nrm_ready, done(g[2]))
                act.wait_ge(o_ready, reuse(g[2] + 3 * NG, 4))
                nc.scalar.activation(nr2[:, g[1], :], nrm[:, g[1], :], ACT.Sqrt).then_inc(nsd_ready, 1)

            pipeline(nc.scalar, [(last_q, 2), (last_s, 0), (last_r, -1)])

        @block.tensor
        def _(pe):
            for s_ in (t_done, root_done, h_done, m_done, a_done, sc_done, q_done, f_done, sq_used):
                pe.sem_inc(s_, OFF)
            pe.wait_ge(made, 7)
            pe.wait_ge(consts_in, 16 * CONSTS)
            pe.wait_ge(tot_ready, 1)
            nc.tensor.matmul(psM[0][0:EP, 0:R], lhsT=before[0:EP, 0:EP], rhs=rowtot, start=True, stop=True)
            nc.tensor.matmul(psM[1][:, 0:R], lhsT=ones[0:EP, :], rhs=rowtot, start=True, stop=True).then_inc(tot_done, 1)

            def node_t(name, g):
                s = g[1] % 2
                if name == "root1":
                    n = g[2]
                    pe.wait_ge(hrow_ready, done(g[2]))
                    rows_ = hrow[:, s, :]
                else:
                    n = ROOT[{"pool": "last"}.get(name, name)] * NG + g[2]
                    pe.wait_ge(x_in[g[1]], x_value(name, g, g[1]))
                    rows_ = X[:, g[1], :]
                if name in ("root1", "pool"):
                    pe.wait_ge(hT_ready, reuse(n, 2))
                else:
                    pe.wait_ge(pre_ready, reuse(n - NG, 2))
                for k in range(T):
                    last = nc.tensor.transpose(psT[s][:, k * P:(k + 1) * P], four(rows_)[:, k, :], ident[:, :])
                last.then_inc(t_done, 1)

            def node_r(l, g):
                s = g[1] % 2
                n = (l - 1) * NG + g[2]
                pe.wait_ge(hT_ready, done(n))
                pe.wait_ge(o_ready, reuse(n, 2))
                for k in range(T):
                    last = nc.tensor.matmul(psO[s][:, k * D:(k + 1) * D], lhsT=hT[:, s, k * P:(k + 1) * P], rhs=root[l][:, :],
                                            start=True, stop=True)
                last.then_inc(root_done, 1)

            def edge_s(l, c, s, b):
                n = 2 * NCH * (l - 1) + c * 2 + b
                if b == 0:
                    pe.wait_ge(g_ready, done(NCH * (l - 1) + c))
                    pe.wait_ge(s_ready, done(NCH * (l - 1) + c))
                pe.wait_ge(h_out, reuse(n, 2))
                for k in range(T):
                    last = nc.tensor.matmul(psH[b][:, k * P:(k + 1) * P], lhsT=G[:, s * CH + b * T + k, :], rhs=S[:, s, b * T + k, :],
                                            start=True, stop=True)
                last.then_inc(h_done, 1)

            def edge_w(l, c, b, offs_):
                n = 2 * NCH * (l - 1) + c * 2 + b
                pe.wait_ge(h_out, done(n))
                pe.wait_ge(m_out, reuse(n, 2))
                for k in range(T):
                    last = nc.tensor.matmul(psM[b][:, k * D:(k + 1) * D], lhsT=HT[:, b, k * P:(k + 1) * P],
                                            rhs=W[l][:, bass.ds(offs_[b * T + k], D)], start=True, stop=True)
                last.then_inc(m_done, 1)

            def offsets(c):
                return [nc.tensor.value_load(woff[0:1, bass.ds(c * CH + k, 1)], min_val=0, max_val=(R - 1) * D) for k in range(CH)]

            pipeline(nc.tensor, [(lambda g: node_t("root1", g), 1), (lambda g: node_r(1, g), 0)])

            pe.wait_ge(car_ready, 1)
            for k in range(2):
                last = nc.tensor.transpose(psM[0][0:1, k * P:k * P + RP], ca[:, k:k + 1], ident[0:RP, 0:RP])
            last.then_inc(car_done, 1)
            pe.wait_ge(car2_ready, 1)
            for k in range(2):
                last = nc.tensor.matmul(psM[1][0:RP, k:k + 1], lhsT=tr[0:1, k * P:k * P + RP], rhs=ones[0:1, 0:1], start=True, stop=True)
            last.then_inc(car2_done, 1)
            pe.wait_ge(slot_ready, 1)
            for n, (h, nm) in enumerate([(h, a) for a in ("srcR", "toR", "repR", "invR") for h in range(2)]):
                if n >= 2:
                    pe.wait_ge(slot_out, n - 1)
                nc.tensor.transpose(psT[n % 2][:, 0:RP], v[nm][:, h * P:(h + 1) * P], ident[0:RP, 0:RP]).then_inc(slot_done, 1)
            for h in range(2):
                last = nc.tensor.transpose(psM[0][0:1, h * P:h * P + RP], v["keyR"][:, h * P:h * P + 1], ident[0:RP, 0:RP])
            last.then_inc(slot_done, 1)

            pe.wait_ge(edges_ready, 1)
            for l in (1, 2, 3):
                if l == 1:
                    with nc.tensor.Fori(0, NCH // 2) as i:
                        for s in range(2):
                            c = i * 2 + s
                            o_ = offsets(c)
                            edge_s(1, c, s, 0)
                            edge_s(1, c, s, 1)
                            edge_w(1, c, 0, o_)
                            edge_w(1, c, 1, o_)
                else:
                    pe.wait_ge(bn_ready, l - 1)

                    def chunk(c, s, groups):
                        o_ = offsets(c)
                        todo = [("t", 0), ("t", 1), ("s", 0), ("r", 0), ("t", 2), ("w", 0), ("r", 1), ("t", 3), ("s", 1), ("r", 2), ("w", 1), ("r", 3)]
                        for what, k in todo:
                            if what == "s":
                                edge_s(l, c, s, k)
                            elif what == "w":
                                edge_w(l, c, k, o_)
                            elif k < len(groups):
                                node_t(f"root{l}", groups[k]) if what == "t" else node_r(l, groups[k])

                    with nc.tensor.Fori(0, GL // 2) as i:
                        for s in range(2):
                            c = i * 2 + s
                            chunk(c, s, [(c, k, c * T + k, False) for k in range(T)])
                    chunk(GL, 0, [LAST[0]])
                    chunk(GL + 1, 1, [LAST[1]])

                pe.wait_ge(heads_in, 16 * l)
                if l == 1:
                    pe.wait_ge(hT_ready, done(NG - 1))
                else:
                    pe.wait_ge(pre_ready, done((l - 1) * NG - 1))
                for h2 in range(2):
                    for h in range(2):
                        last = nc.tensor.matmul(psT[h2][0:RP, 0:D], lhsT=fixS[:, h, h2, :], rhs=fixin[:, h * P:(h + 1) * P],
                                                start=(h == 0), stop=(h == 1))
                    last.then_inc(fix_done, 1)

                if l < 3:
                    pe.wait_ge(m_out, done(2 * NCH * l - 1))
                    pe.wait_ge(hbar_ready, l)
                    nc.tensor.matmul(psH[1][:, 0:D], lhsT=hbarw[:, :], rhs=root[l][:, :], start=True, stop=True)
                    nc.tensor.matmul(psH[0][:, :], lhsT=ones[:, :], rhs=MF[:, 0:T * D], start=True, stop=False)
                    with nc.tensor.Fori(1, NT // T - 1) as i:
                        nc.tensor.matmul(psH[0][:, :], lhsT=ones[:, :], rhs=MF[:, bass.ds(i * (T * D), T * D)], start=False, stop=False)
                    nc.tensor.matmul(psH[0][:, :], lhsT=ones[:, :], rhs=MF[:, (NT - T) * D:NT * D], start=False, stop=True).then_inc(msum_done, 1)

                    def squares(g):
                        n = (l - 1) * NG + g[2]
                        pe.wait_ge(sq_ready, done(n))
                        kp, w = (TAIL_P, TAIL_T * D) if g[3] else (P, GROUP)
                        nc.tensor.matmul(psM[0][:, 0:w], lhsT=ones[0:kp, :], rhs=hpre[0:kp, g[1] % 2, 0:w], start=isinstance(g[2], int) and g[2] == 0,
                                         stop=g[3]).then_inc(sq_used, 1)
                    pipeline(nc.tensor, [(squares, 0)])
                    pe.wait_ge(bn_rows, l)
                    nc.tensor.transpose(psM[1][:, 0:P], scale[:, :], ident[:, :])
                    nc.tensor.transpose(psM[1][:, P:2 * P], shift[:, :], ident[:, :]).then_inc(col_done, 1)

            def pool_a(g):
                pe.wait_ge(hT_ready, done(g[2] + 3 * NG))
                pe.wait_ge(z_ready, reuse(g[2], 2))
                nc.tensor.matmul(psO[g[1] % 2][0:D // 2, :], lhsT=A1[:, :], rhs=embT(g[1]), start=True, stop=True).then_inc(a_done, 1)

            def pool_c(g):
                pe.wait_ge(q_out, reuse(g[2], 2))
                nc.tensor.matmul(psM[g[1] % 2][:, :], lhsT=C1[:, 0, :], rhs=embT(g[1]), start=True, stop=True).then_inc(q_done, 1)

            def pool_s(g):
                pe.wait_ge(s1_ready, done(g[2]))
                pe.wait_ge(e_ready, reuse(g[2], 2))
                nc.tensor.matmul(psH[g[1] % 2][:, :], lhsT=A2rep[:, :], rhs=S1(g[1]), start=True, stop=True).then_inc(sc_done, 1)

            pe.wait_ge(o_ready, done(3 * NG - 1))
            pipeline(nc.tensor, [(lambda g: node_t("pool", g), 1), (pool_a, 0), (pool_c, 0), (pool_s, -1)])

            pe.wait_ge(pool_ready, 2)
            nc.tensor.matmul(psM[0][:, 0:1], lhsT=C1[:, 1, :], rhs=small[:, 3:4], start=True, stop=True).then_inc(pool_done, 1)

            def last_c(g):
                pe.wait_ge(f_ready, done(g[2]))
                pe.wait_ge(fin_ready, reuse(g[2], 2))
                for k in range(T):
                    last = nc.tensor.matmul(psO[g[1] % 2][:, k * D:(k + 1) * D], lhsT=hT[:, g[1] % 2, k * P:(k + 1) * P], rhs=C2[:, :],
                                            start=True, stop=True)
                last.then_inc(f_done, 1)
            pipeline(nc.tensor, [(last_c, 0)])

        @block.vector
        def _(dve):
            ch = Chain(dve, dve_chain)
            V = nc.vector
            for s_ in (o_ready, hrow_ready, hT_ready, g_ready, ln_ready, s_ready, cen_ready, s1_ready, max_ready, w_done, f_ready, fin_ready, nrm_ready,
                       xv_ready, lnv_ready):
                dve.sem_inc(s_, OFF)
            V.memset(z0, 0.0)
            V.memset(hsum[:, :], 0.0)
            V.memset(O[:, :, :], 0.0).then_inc(spare0, 1)
            ch.mark(V.memset(pad_i, 0))
            ch.wait()
            V.memset(pad_i.rearrange("p (s two) -> p s two", two=2)[:, :, 0], R * KEY).then_inc(pads_made, 1)
            dve.wait_ge(made, 7)

            dve.wait_ge(edges_in, 48)
            V.tensor_copy(dst_f, dst_i)
            ch.mark(V.tensor_copy(typ_f, typ_i))
            ch.wait()
            for r in range(R):
                V.tensor_scalar(hot[:, r, :], typ_f, float(r), None, ALU.is_equal)
            ch.mark(V.memset(small[:, 13:14], 0.0))
            ch.wait()
            for r in range(R):
                V.tensor_tensor_scan(run[:, r, :], hot[:, r, :], z0, 0.0, ALU.add, ALU.add)
            ch.mark(V.scalar_tensor_tensor(term, typ_f, float(KEY), dst_f, ALU.mult, ALU.add))
            ch.wait()
            V.tensor_copy(recE[:, :, 0], term)
            V.tensor_copy(recE[:, :, 1], src_i)
            V.tensor_copy(rowtot, run[:, :, ET - 1]).then_inc(tot_ready, 1)
            dve.wait_ge(tot_done, 1)
            ch.mark(V.tensor_scalar(toti, psM[1][:, 0:R], float(P - 1), None, ALU.add))
            ch.wait()
            ch.mark(V.tensor_scalar(toti, toti, 7, 7, ALU.logical_shift_right, ALU.logical_shift_left))
            ch.wait()
            ch.mark(V.tensor_copy(tot, toti))
            ch.mark(V.memset(tbase[:, 0:1], 0.0))
            ch.wait()
            for r in range(1, R):
                ch.mark(V.tensor_tensor(tbase[:, r:r + 1], tbase[:, r - 1:r], tot[:, r - 1:r], ALU.add))
                ch.wait()
            ch.mark(V.tensor_tensor(offs, tbase[0:EP, :], psM[0][0:EP, 0:R], ALU.add))
            ch.wait()
            ch.mark(V.scalar_tensor_tensor(pos_f, run[:, 0, :], offs[:, 0:1], hot[:, 0, :], ALU.add, ALU.mult))
            for r in range(1, R):
                ch.mark(V.scalar_tensor_tensor(term, run[:, r, :], offs[:, r:r + 1], hot[:, r, :], ALU.add, ALU.mult))
                ch.wait()
                ch.mark(V.tensor_tensor(pos_f, pos_f, term, ALU.add))
                ch.wait()
            V.tensor_copy(posI, pos_f).then_inc(pos_ready, 1)
            dve.wait_ge(consts_in, 16 * CONSTS)
            ch.mark(V.tensor_copy(A2rep[:, :], A2[:, 0:1].to_broadcast([D // 2, P])))

            def stat_x(g):
                s = g[1] % 2
                dve.wait_ge(x_in[g[1]], x_value("root1", g, g[1]))
                dve.wait_ge(hrow_ready, reuse(g[2], 2))
                for k in range(T):
                    last = V.bn_stats(xst[:, s, k, :], four(X[:, g[1], :])[:, k, :])
                ch.mark(last)
                ch.wait()
                dve.sem_inc(passed)
                for k in range(T):
                    last = V.bn_aggr(xmv[:, s, k, :], xst[:, s, k, :])
                last.then_inc(xv_ready, 1)

            def norm_x(g):
                s = g[1] % 2
                dve.wait_ge(xs_ready, done(g[2]))
                ch.mark(V.reciprocal(xr[:, s, :], xsd[:, s, :]))
                ch.wait()
                dve.wait_ge(t_done, reuse(g[2], 2))
                for k in range(T):
                    last = V.tensor_scalar(four(hrow[:, s, :])[:, k, :], four(X[:, g[1], :])[:, k, :], xmv[:, s, k, 0:1], xr[:, s, k:k + 1],
                                           ALU.subtract, ALU.mult)
                last.then_inc(hrow_ready, 1)

            def lrelu(l, g):
                n = (l - 1) * NG + g[2]
                s = g[1] % 2
                dve.wait_ge(pre_ready, done(n - NG))
                dve.wait_ge(root_done, reuse(n, 2))
                a = cols(hpre[:, s, :], g[3])
                V.scalar_tensor_tensor(cols(hT[:, s, :], g[3]), a, SLOPE, a, ALU.mult, ALU.max,
                                       accum_out=hsum[:, bass.ds(g[2], 1)]).then_inc(hT_ready, 1)

            def bias(l, g):
                n = (l - 1) * NG + g[2]
                dve.wait_ge(root_done, done(n))
                dve.wait_ge(o_stored[g[1]], o_value(f"root{l}", g, g[1]))
                V.tensor_tensor(four(O[:, g[1], :]), four(psO[g[1] % 2][:, :]), rep4(brow[l]), ALU.add).then_inc(o_ready, 1)

            pipeline(V, [(stat_x, 2), (norm_x, 1), (lambda g: bias(1, g), 0)], ch, 2)

            dve.wait_ge(rec_in, 48)
            key, prv, nxt = v["keyR"], v["prevR"], v["nextR"]
            V.tensor_copy(prv, rec3[0][:, :, 0])
            V.tensor_copy(key, rec3[1][:, :, 0])
            V.tensor_copy(nxt, rec3[2][:, :, 0])
            V.tensor_copy(keyi, rec3[1][:, :, 0])
            ch.mark(V.tensor_copy(v["srcR"], rec3[1][:, :, 1]))
            ch.wait()
            slot = v["slotR"]
            V.tensor_tensor(v["firstR"], key, prv, ALU.not_equal)
            V.tensor_tensor(v["w0"], key, nxt, ALU.not_equal)
            V.tensor_scalar(v["realR"], key, float(R * KEY), None, ALU.is_lt)
            ch.mark(V.tensor_scalar(lowi, keyi, KEY - 1, None, ALU.bitwise_and))
            ch.wait()
            V.tensor_copy(v["dstR"], lowi)
            ch.mark(V.tensor_tensor(v["w1"], v["firstR"], slot, ALU.mult))
            ch.wait()
            ch.mark(V.tensor_tensor_scan(v["rs"], v["w1"], v["w1"], 0.0, ALU.max, ALU.max))
            ch.mark(V.tensor_scalar(v["nf"], slot, -float(SLOTS), None, ALU.add))
            ch.wait()
            ch.mark(V.tensor_tensor(v["re"], v["nf"], v["w0"], ALU.mult))
            ch.wait()
            a, b = v["re"], v["nf"]
            for d in (1, 2, 4, 8, 16, 32, 64, 128):
                V.tensor_tensor(b[:, 0:L2 - d], a[:, 0:L2 - d], a[:, d:L2], ALU.min)
                ch.mark(V.tensor_copy(b[:, L2 - d:L2], a[:, L2 - d:L2]))
                ch.wait()
                a, b = b, a
            re = a
            V.tensor_copy(ca[:, 0:1], v["rs"][:, L2 - 1:L2])
            V.tensor_copy(ca[:, 1:2], re[:, 0:1]).then_inc(car_ready, 1)
            dve.wait_ge(car_done, 1)
            c0, c1_ = tr[0:1, 0:RP], tr[0:1, P:P + RP]
            ch.mark(V.tensor_copy(trow[0:1, 0:RP], psM[0][0:1, 0:RP]))
            ch.mark(V.tensor_copy(trow[0:1, P:P + RP], psM[0][0:1, P:P + RP]))
            ch.mark(V.memset(tr[0:1, :], 0.0))
            ch.wait()
            ch.mark(V.tensor_tensor_scan(tr[0:1, 1:RP], trow[0:1, 0:RP - 1], trow[0:1, 0:RP - 1], 0.0, ALU.max, ALU.max))
            a, b = trow[0:1, P:P + RP], trow[0:1, 2 * P:2 * P + RP]
            for d in (1, 2, 4, 8, 16, 32, 64):
                V.tensor_tensor(b[:, 0:RP - d], a[:, 0:RP - d], a[:, d:RP], ALU.min)
                ch.mark(V.tensor_copy(b[:, RP - d:RP], a[:, RP - d:RP]))
                ch.wait()
                a, b = b, a
            V.tensor_copy(tr[0:1, P:P + RP - 1], a[:, 1:RP]).then_inc(car2_ready, 1)
            dve.wait_ge(car2_done, 1)
            ch.mark(V.tensor_copy(ca[:, 2:4], psM[1][0:RP, 0:2]))
            ch.wait()
            ch.mark(V.tensor_scalar(v["rs"], v["rs"], ca[:, 2:3], None, ALU.max))
            ch.mark(V.tensor_scalar(v["w1"], re, 0.0, ca[:, 3:4], ALU.is_equal, ALU.mult))
            ch.wait()
            ch.mark(V.tensor_tensor(re, re, v["w1"], ALU.add))
            ch.wait()
            ch.mark(V.scalar_tensor_tensor(v["w1"], re, float(SLOTS + 1), v["rs"], ALU.add, ALU.subtract))
            V.tensor_scalar(v["tsR"][:, 0:P], slot[:, 0:1].to_broadcast([RP, P]), 0.0, None, ALU.add)
            ch.mark(V.tensor_scalar(v["tsR"][:, P:L2], slot[:, P:P + 1].to_broadcast([RP, P]), 0.0, None, ALU.add))
            ch.wait()
            ch.mark(V.reciprocal(v["invR"], v["w1"]))
            ch.mark(V.tensor_tensor(v["w0"], v["rs"], v["tsR"], ALU.max))
            ch.wait()
            ch.mark(V.scalar_tensor_tensor(v["w1"], v["w0"], 1.0, v["tsR"], ALU.add, ALU.subtract))
            ch.wait()
            ch.mark(V.tensor_tensor(v["w1"], v["w1"], v["realR"], ALU.mult))
            ch.wait()
            ch.mark(V.tensor_scalar(v["repR"], v["w1"], -1.0, None, ALU.add))
            ch.wait()
            ch.mark(V.tensor_tensor(v["w0"], v["firstR"], v["realR"], ALU.mult))
            ch.mark(V.tensor_scalar(v["w1"], slot, float(N), None, ALU.add))
            ch.wait()
            ch.mark(V.tensor_tensor(v["toR"], v["dstR"], v["w1"], ALU.subtract))
            ch.wait()
            ch.mark(V.tensor_tensor(v["toR"], v["toR"], v["w0"], ALU.mult))
            ch.wait()
            ch.mark(V.tensor_tensor(v["toR"], v["toR"], v["w1"], ALU.add))
            ch.wait()
            h0 = lambda ap: ap.rearrange("q (h s) -> q h s", h=2)[:, :, 0]
            ch.mark(V.tensor_tensor(fv, h0(v["rs"]), h0(v["tsR"]), ALU.is_lt))
            ch.wait()
            ch.mark(V.tensor_tensor(fv, fv, h0(v["realR"]), ALU.mult))
            ch.wait()
            ch.mark(V.tensor_tensor(fk, h0(v["dstR"]), jR, ALU.add))
            ch.wait()
            ch.mark(V.tensor_scalar(fk, fk, 1.0, None, ALU.add))
            ch.wait()
            ch.mark(V.tensor_tensor(fk, fk, fv, ALU.mult))
            ch.wait()
            ch.mark(V.tensor_tensor(fk, fk, jR, ALU.subtract))
            ch.wait()
            V.tensor_scalar(fk2[:, 0:2], fk, -1.0, None, ALU.add).then_inc(hk_ready, 1)
            dve.wait_ge(hk_ready, 1)
            V.tensor_copy(small[:, 12:13], small[:, 13:14]).then_inc(slot_ready, 1)
            dve.wait_ge(slot_done, 9)
            for h in range(2):
                last = V.tensor_copy(trowi[0:1, h:NT:2], psM[0][0:1, h * P:h * P + RP])
            ch.mark(last)
            ch.wait()
            ch.mark(V.tensor_scalar(trowi, trowi, 16, None, ALU.logical_shift_right))
            ch.wait()
            ch.mark(V.tensor_copy(trow[0:1, 0:NT], trowi))
            ch.wait()
            V.tensor_scalar(woff[0:1, :], trow[0:1, 0:NT], float(R - 1), float(D), ALU.min, ALU.mult)
            ch.mark(V.memset(trow[0:1, NT:NT + 1], 0.0))
            ch.mark(V.tensor_tensor(trow[0:1, NT + 1:2 * NT], trow[0:1, 1:NT], trow[0:1, 0:NT - 1], ALU.not_equal))
            ch.mark(V.tensor_copy(trow[0:1, 2 * NT:3 * NT].rearrange("o (c k) -> o c k", k=CH),
                                  jall[0:1, 0:CH].unsqueeze(1).to_broadcast([1, NCH, CH])))
            ch.wait()
            V.scalar_tensor_tensor(same[0:1, :], trow[0:1, 2 * NT:3 * NT], 16.0, trow[0:1, NT:2 * NT], ALU.mult, ALU.mult)
            ch.mark(V.tensor_scalar(other[0:1, :], trow[0:1, NT:2 * NT], float(16 * CH), None, ALU.mult))
            dve.wait_ge(hk_in, 16)
            for h in range(2):
                ch.mark(V.tensor_scalar(fe[:, h, :], fkall[0:RP, :], fk2[:, h:h + 1], float(NT), ALU.not_equal, ALU.mult))
            ch.wait()
            for h in range(2):
                ch.mark(V.tensor_tensor(fe[:, h, :], fe[:, h, :], jall[0:RP, :], ALU.add))
            ch.wait()
            for h in range(2):
                ch.mark(V.tensor_reduce(frep[:, h:h + 1], fe[:, h, :], AX.X, ALU.min))
            ch.wait()
            for h in range(2):
                last = V.tensor_scalar(fixS[:, h, :, :].rearrange("q b c -> q c b"), jall[0:RP, :].rearrange("q (c b) -> q c b", b=2),
                                       frep[:, h:h + 1], fv[:, h:h + 1], ALU.is_equal, ALU.mult)
            ch.mark(last)
            ch.mark(V.tensor_tensor(fk2[:, 2:4], frep, jR, ALU.is_equal))
            ch.mark(V.tensor_scalar(fk2[:, 4:6], jR, float(P), float(N), ALU.mult, ALU.add))
            ch.wait()
            ch.mark(V.tensor_tensor(fk2[:, 2:4], fk2[:, 2:4], fv, ALU.mult))
            ch.mark(V.tensor_tensor(fk2[:, 6:8], h0(v["dstR"]), fk2[:, 4:6], ALU.subtract))
            ch.wait()
            ch.mark(V.tensor_tensor(fk2[:, 6:8], fk2[:, 6:8], fk2[:, 2:4], ALU.mult))
            ch.wait()
            ch.mark(V.tensor_tensor(fixto[:, :], fk2[:, 6:8], fk2[:, 4:6], ALU.add))
            ch.wait()
            dve.wait_ge(slot_out, 8)
            dve.sem_inc(edges_ready)

            def build_s(l, c, s):
                dve.wait_ge(h_done, reuse(2 * NCH * (l - 1) + c * 2 + 1, 4))
                for k in range(CH):
                    j = c * CH + k
                    last = V.tensor_scalar(S[:, s, k, :], iota[:, :], repA[:, bass.ds(j, 1)], invA[:, bass.ds(j, 1)], ALU.is_equal, ALU.mult)
                last.then_inc(s_ready, 1)

            def norm_g1(c, n, s):
                dve.wait_ge(gath[s], n * (16 * CH) + 16 * CH)
                for k in range(CH):
                    last = V.bn_stats(lnst[:, k, :], G[:, s * CH + k, :])
                ch.mark(last)
                ch.wait()
                dve.wait_ge(g_ready, reuse(c, 2))
                dve.sem_inc(passed)
                for k in range(CH):
                    last = V.bn_aggr(lnmv[:, s, k, :], lnst[:, k, :])
                last.then_inc(lnv_ready, 1)
                dve.wait_ge(lns_ready, done(c))
                ch.mark(V.reciprocal(lnr[:, s, :], lnsd[:, s, :]))
                ch.wait()
                V.scalar_tensor_tensor(lnb[:, s, :], lnmv[:, s, :, 0], -1.0, lnr[:, s, :], ALU.mult, ALU.mult).then_inc(ln_ready, 1)

            def norm_g(l, c, n, s):
                dve.wait_ge(gath[s], (NCH // 2) * (16 * CH) * (l - 1) + n * (16 * CH) + 16 * CH)
                g8 = G[:, s * CH:(s + 1) * CH, :]
                rep8 = lambda ap: ap[:, :].unsqueeze(1).to_broadcast([P, CH, D])
                ch.mark(V.tensor_tensor(g8, g8, rep8(scale), ALU.mult))
                ch.wait()
                ch.mark(V.tensor_tensor(g8, g8, rep8(shift), ALU.add))
                ch.wait()
                V.scalar_tensor_tensor(g8, g8, SLOPE, g8, ALU.mult, ALU.max).then_inc(g_ready, 1)

            for l in (1, 2, 3):
                if l == 1:
                    with V.Fori(0, NCH // 2) as i:
                        ch.enter(i, 4)
                        for s in range(2):
                            build_s(1, i * 2 + s, s)
                            norm_g1(i * 2 + s, i, s)
                        ch.leave(NCH // 2)
                else:
                    def chunk(c, n, s, groups):
                        build_s(l, c, s)
                        norm_g(l, c, n, s)
                        for k in range(len(groups) + 1):
                            if k < len(groups):
                                lrelu(l, groups[k])
                            if k > 0:
                                bias(l, groups[k - 1])

                    with V.Fori(0, GL // 2) as i:
                        ch.enter(i, 4)
                        for s in range(2):
                            c = i * 2 + s
                            chunk(c, i, s, [(c, k, c * T + k, False) for k in range(T)])
                        ch.leave(GL // 2)
                    chunk(GL, GL // 2, 0, [LAST[0]])
                    chunk(GL + 1, GL // 2, 1, [LAST[1]])

                if l == 3:
                    break
                dve.wait_ge(hT_ready, done(NG * l - 1))
                ch.mark(V.tensor_reduce(hbar[:, :], hsum[:, :], AX.X, ALU.add))
                ch.wait()
                V.tensor_copy(hbarw[:, :], hbar[:, 0:1].to_broadcast([P, P])).then_inc(hbar_ready, 1)
                dve.wait_ge(msum_done, l)
                ch.mark(V.tensor_reduce(tmp[:, :], psH[0][:, :].rearrange("p (t d) -> p d t", t=T), AX.X, ALU.add))
                ch.wait()
                ch.mark(V.tensor_tensor(tmp[:, :], tmp[:, :], psH[1][:, 0:D], ALU.add))
                ch.wait()
                ch.mark(V.scalar_tensor_tensor(mean[:, :], tmp[:, :], 1.0 / N, brow[l][:, :], ALU.mult, ALU.add))
                ch.wait()

                def centre(g):
                    n = (l - 1) * NG + g[2]
                    dve.wait_ge(x_in[g[1]], x_value(f"stat{l}", g, g[1]))
                    dve.wait_ge(sq_ready, reuse(n, 2))
                    V.tensor_tensor(four(hrow[:, g[1] % 2, :]), four(X[:, g[1], :]), rep4(mean), ALU.subtract).then_inc(cen_ready, 1)
                pipeline(V, [(centre, 0)])
                dve.wait_ge(sq_used, done(NG * l - 1))
                ch.mark(V.tensor_reduce(tmp[:, :], psM[0][:, :].rearrange("p (t d) -> p d t", t=T), AX.X, ALU.add))
                ch.wait()
                V.tensor_scalar(var[:, :], tmp[:, :], 1.0 / N, EPS, ALU.mult, ALU.add).then_inc(var_ready, 1)
                dve.wait_ge(sd_ready, l)
                ch.mark(V.reciprocal(tmp2[:, :], tmp2[:, :]))
                ch.wait()
                ch.mark(V.tensor_tensor(scale[:, :], tmp2[:, :], grow[l][:, :], ALU.mult))
                ch.wait()
                ch.mark(V.tensor_tensor(tmp[:, :], mean[:, :], scale[:, :], ALU.mult))
                ch.wait()
                V.tensor_tensor(shift[:, :], betarow[l][:, :], tmp[:, :], ALU.subtract).then_inc(bn_rows, 1)
                dve.wait_ge(col_done, l)
                V.tensor_copy(scol[:, :], psM[1][:, 0:1])
                V.tensor_copy(bcol[:, :], psM[1][:, P:P + 1]).then_inc(bn_ready, 1)
                dve.wait_ge(bn_ready, l)

            def pool_s1(g):
                dve.wait_ge(z_ready, done(g[2]))
                z = hrow[0:D // 2, g[1] % 2, :]
                dve.wait_ge(sc_done, reuse(g[2], 4))
                V.scalar_tensor_tensor(S1(g[1]), z, SLOPE, z, ALU.mult, ALU.max).then_inc(s1_ready, 1)

            def pool_max(g):
                dve.wait_ge(sc_done, done(g[2]))
                c = bass.ds(g[2], 1)
                ch.mark(V.tensor_reduce(gmax[:, c], cols(psH[g[1] % 2][:, :], g[3]), AX.XY, ALU.max))
                ch.wait()
                V.tensor_scalar(nbias[:, c], gmax[:, c], -1.0, None, ALU.mult).then_inc(max_ready, 1)

            def pool_w(g):
                dve.wait_ge(e_ready, done(g[2]))
                V.scalar_tensor_tensor(cols(X4(g[1] % 2), g[3]), cols(EX(g[1]), g[3]), 1.0, cols(embT(g[1]), g[3]), ALU.mult, ALU.mult,
                                       accum_out=wsum[:, bass.ds(g[2], 1)]).then_inc(w_done, 1)

            pipeline(V, [(pool_s1, 0), (pool_max, -1), (pool_w, -2)], ch, 1)
            ch.mark(V.tensor_scalar(gmax[:, :], gmax[:, :], a2[:, 0:1], None, ALU.add))
            ch.wait()
            ch.mark(V.tensor_reduce(small[:, 1:2], gmax[:, :], AX.X, ALU.max))
            ch.wait()
            V.tensor_scalar(small[:, 0:1], small[:, 1:2], -1.0, None, ALU.mult).then_inc(pool_ready, 1)
            dve.wait_ge(pool_done, 1)
            ch.mark(V.tensor_tensor(esum[:, :], esum[:, :], hsum[:, :], ALU.mult))
            ch.mark(V.tensor_tensor(wsum[:, :], wsum[:, :], hsum[:, :], ALU.mult))
            ch.wait()
            ch.mark(V.tensor_reduce(small[:, 5:6], esum[:, :], AX.X, ALU.add))
            ch.mark(V.tensor_reduce(small[:, 6:7], wsum[:, :], AX.X, ALU.add))
            ch.wait()
            ch.mark(V.reciprocal(small[:, 7:8], small[:, 5:6]))
            ch.wait()
            V.tensor_tensor(small[:, 3:4], small[:, 6:7], small[:, 7:8], ALU.mult).then_inc(pool_ready, 1)
            dve.wait_ge(pool_done, 2)
            V.tensor_tensor(small[:, 4:5], psM[0][:, 0:1], c1[:, :], ALU.add).then_inc(qb_ready, 1)

            def last_f(g):
                dve.wait_ge(f_pre, done(g[2]))
                dve.wait_ge(f_done, reuse(g[2], 2))
                a = hpre[:, g[1] % 2, :]
                V.scalar_tensor_tensor(hT[:, g[1] % 2, :], a, SLOPE, a, ALU.mult, ALU.max).then_inc(f_ready, 1)

            def last_b(g):
                dve.wait_ge(f_done, done(g[2]))
                V.tensor_tensor(four(FIN(g[1])), four(psO[g[1] % 2][:, :]), rep4(c2row), ALU.add).then_inc(fin_ready, 1)

            def last_m(g):
                dve.wait_ge(ss_ready, done(g[2]))
                V.tensor_scalar(nrm[:, g[1], :], nrm[:, g[1], :], 1e-24, None, ALU.max).then_inc(nrm_ready, 1)

            def last_o(g):
                k4 = g[1]
                dve.wait_ge(nsd_ready, done(g[2]))
                ch.mark(V.reciprocal(nrm2[:, k4, :], nr2[:, k4, :]))
                ch.wait()
                dve.wait_ge(x_in[k4], x_value("last", g, k4))
                dve.wait_ge(o_stored[k4], o_value("last", g, k4))
                for k in range(T):
                    last = V.scalar_tensor_tensor(four(O[:, k4, :])[:, k, :], four(FIN(k4))[:, k, :], nrm2[:, k4, k:k + 1],
                                                  four(X[:, k4, :])[:, k, :], ALU.mult, ALU.add)
                last.then_inc(o_ready, 1)

            pipeline(V, [(last_f, 1), (last_b, 0), (last_m, -1), (last_o, -2)], ch, 1)


INPUTS = ["x", "src", "dst", "edge_type_8"] + ["L0_gnn_" + n for n in
          ("W1", "root1", "b1", "W2", "root2", "b2", "W3", "root3", "b3", "g1", "beta1", "g2", "beta2",
           "A1", "a1", "A2", "a2", "C1", "c1", "C2", "c2")]


def kernel(**inputs):
    import numpy as np
    import concourse.bacc as bacc
    from concourse.bass_utils import run_bass_kernel_spmd

    nc = bacc.Bacc("TRN2", target_bir_lowering=False, num_devices=1)
    arrays, t = {}, {}
    for name in INPUTS:
        a = np.ascontiguousarray(inputs[name])
        arrays["in_" + name] = a
        t[name] = nc.dram_tensor("in_" + name, a.shape, mybir.dt.from_np(a.dtype), kind="ExternalInput").ap()
    out = nc.dram_tensor("result", (N, D), F32, kind="ExternalOutput").ap()
    gnn_program(nc, t, out)
    r = run_bass_kernel_spmd(nc, [arrays], core_ids=[0])
    return r.results[0]["result"]
```
